# Optimizing a Trainium2 kernel written in Bass

```python
import numpy as np
import jax
import jax.numpy as jnp

def _softmax(x, axis=-1):
    return jax.nn.softmax(x, axis=axis)

def _gelu(x):
    return jax.nn.gelu(x, approximate=True)

def _silu(x):
    return jax.nn.silu(x)

def _sigmoid(x):
    return jax.nn.sigmoid(x)

def _layernorm(x, axis=-1, eps=1e-05):
    m = jnp.mean(x, axis=axis, keepdims=True)
    v = jnp.var(x, axis=axis, keepdims=True)
    return (x - m) / jnp.sqrt(v + eps)

def _scatter_add(tgt, idx, src, axis=0):
    return tgt.at[idx].add(src)

def _segment_sum(src, seg, n):
    return jax.ops.segment_sum(src, seg, n)
kernel_name = 'mk_rec_standalone_d1_rec_r8_54cc5c'

def setup_inputs(seed: int=0):
    np.random.seed(seed)
    _w = jnp.asarray

    def _rec_inputs():
        import jax
        import jax.numpy as jnp
        _rk = jax.random.key(seed)
        r_emb = -0.000718957 + 1.00057 * jax.random.normal(jax.random.fold_in(_rk, 1), (2048, 320), jnp.float32)
        return r_emb
    r_emb = _rec_inputs()

    def _L0_rec_setup():
        import itertools
        import jax, jax.numpy as jnp
        import numpy as np
        F_FIELDS = 40
        E = 8
        REDUCTION = max(1, F_FIELDS // 8)
        N_PAIRS = F_FIELDS * (F_FIELDS - 1) // 2
        DNN_IN = F_FIELDS * (F_FIELDS - 1) * E
        BN_EPS = 1e-05
        _pairs = np.array(list(itertools.combinations(range(F_FIELDS), 2)), dtype=np.int32)
        PAIR_I = jnp.asarray(_pairs[:, 0])
        PAIR_J = jnp.asarray(_pairs[:, 1])

        def _bilinear_all(V, w_bl):
            t = jnp.einsum('bfe,de->bfd', V, w_bl)
            return t[:, PAIR_I] * V[:, PAIR_J]
        key = jax.random.key(seed)
        ks = jax.random.split(key, 16)
        B = 1024
        emb = jax.random.normal(ks[0], (B, F_FIELDS * E), jnp.float32)
        bn_weight = jnp.ones((F_FIELDS * E,), jnp.float32) + 0.05 * jax.random.normal(ks[1], (F_FIELDS * E,), jnp.float32)
        bn_bias = 0.05 * jax.random.normal(ks[2], (F_FIELDS * E,), jnp.float32)
        bn_mean = 0.1 * jax.random.normal(ks[3], (F_FIELDS * E,), jnp.float32)
        bn_var = jnp.ones((F_FIELDS * E,), jnp.float32) + 0.1 * jax.random.uniform(ks[4], (F_FIELDS * E,), jnp.float32)
        se_w1 = 0.1 * jax.random.normal(ks[5], (REDUCTION, F_FIELDS), jnp.float32)
        se_w2 = 0.1 * jax.random.normal(ks[6], (F_FIELDS, REDUCTION), jnp.float32)
        w_bl = 0.3 * jax.random.normal(ks[7], (E, E), jnp.float32)
        d_w1 = 0.02 * jax.random.normal(ks[8], (1024, DNN_IN), jnp.float32)
        d_b1 = jnp.zeros((1024,), jnp.float32)
        d_w2 = 0.02 * jax.random.normal(ks[9], (512, 1024), jnp.float32)
        d_b2 = jnp.zeros((512,), jnp.float32)
        d_w3 = 0.02 * jax.random.normal(ks[10], (1, 512), jnp.float32)
        d_b3 = jnp.zeros((1,), jnp.float32)
        return {'emb': emb, 'bn_weight': bn_weight, 'bn_bias': bn_bias, 'bn_mean': bn_mean, 'bn_var': bn_var, 'se_w1': se_w1, 'se_w2': se_w2, 'w_bl': w_bl, 'd_w1': d_w1, 'd_b1': d_b1, 'd_w2': d_w2, 'd_b2': d_b2, 'd_w3': d_w3, 'd_b3': d_b3}
    _L0_rec_all = _L0_rec_setup()
    _L0_rec_in = {k: v for k, v in _L0_rec_all.items() if k in ('bn_weight', 'bn_bias', 'bn_mean', 'bn_var', 'se_w1', 'se_w2', 'w_bl', 'd_w1', 'd_b1', 'd_w2', 'd_b2', 'd_w3', 'd_b3')}
    del _L0_rec_all
    return {'r_emb': r_emb, 'L0_rec_bn_weight': _L0_rec_in['bn_weight'], 'L0_rec_bn_bias': _L0_rec_in['bn_bias'], 'L0_rec_bn_mean': _L0_rec_in['bn_mean'], 'L0_rec_bn_var': _L0_rec_in['bn_var'], 'L0_rec_se_w1': _L0_rec_in['se_w1'], 'L0_rec_se_w2': _L0_rec_in['se_w2'], 'L0_rec_w_bl': _L0_rec_in['w_bl'], 'L0_rec_d_w1': _L0_rec_in['d_w1'], 'L0_rec_d_b1': _L0_rec_in['d_b1'], 'L0_rec_d_w2': _L0_rec_in['d_w2'], 'L0_rec_d_b2': _L0_rec_in['d_b2'], 'L0_rec_d_w3': _L0_rec_in['d_w3'], 'L0_rec_d_b3': _L0_rec_in['d_b3']}

def reference(r_emb, L0_rec_bn_weight, L0_rec_bn_bias, L0_rec_bn_mean, L0_rec_bn_var, L0_rec_se_w1, L0_rec_se_w2, L0_rec_w_bl, L0_rec_d_w1, L0_rec_d_b1, L0_rec_d_w2, L0_rec_d_b2, L0_rec_d_w3, L0_rec_d_b3):
    import jax
    import jax.numpy as jnp

    def _L0_rec_ref(emb, bn_weight, bn_bias, bn_mean, bn_var, se_w1, se_w2, w_bl, d_w1, d_b1, d_w2, d_b2, d_w3, d_b3):
        import itertools
        import jax, jax.numpy as jnp
        import numpy as np
        F_FIELDS = 40
        E = 8
        REDUCTION = max(1, F_FIELDS // 8)
        N_PAIRS = F_FIELDS * (F_FIELDS - 1) // 2
        DNN_IN = F_FIELDS * (F_FIELDS - 1) * E
        BN_EPS = 1e-05
        _pairs = np.array(list(itertools.combinations(range(F_FIELDS), 2)), dtype=np.int32)
        PAIR_I = jnp.asarray(_pairs[:, 0])
        PAIR_J = jnp.asarray(_pairs[:, 1])

        def _bilinear_all(V, w_bl):
            t = jnp.einsum('bfe,de->bfd', V, w_bl)
            return t[:, PAIR_I] * V[:, PAIR_J]
        x = (emb - bn_mean) * jax.lax.rsqrt(bn_var + BN_EPS) * bn_weight + bn_bias
        V0 = x.reshape(x.shape[0], F_FIELDS, E)
        Z = V0.mean(axis=-1)
        A = jax.nn.relu(jax.nn.relu(Z @ se_w1.T) @ se_w2.T)
        Vse = V0 * A[:, :, None]
        p = jnp.concatenate([_bilinear_all(Vse, w_bl), _bilinear_all(V0, w_bl)], axis=1)
        h = p.reshape(p.shape[0], -1)
        h = jax.nn.relu(h @ d_w1.T + d_b1)
        h = jax.nn.relu(h @ d_w2.T + d_b2)
        out = h @ d_w3.T + d_b3
        return jax.nn.sigmoid(out)
    y = _L0_rec_ref(r_emb, L0_rec_bn_weight, L0_rec_bn_bias, L0_rec_bn_mean, L0_rec_bn_var, L0_rec_se_w1, L0_rec_se_w2, L0_rec_w_bl, L0_rec_d_w1, L0_rec_d_b1, L0_rec_d_w2, L0_rec_d_b2, L0_rec_d_w3, L0_rec_d_b3)
    return y

_drawn_inputs = setup_inputs


def setup_inputs(seed=0):
    import zlib

    import numpy as np

    out = dict(_drawn_inputs(seed))
    spreads = {'L0_rec_d_b1': (0.0, 2.0), 'L0_rec_d_b2': (0.0, 1.269)}
    factors = {'L0_rec_bn_weight': 8.0,
     'L0_rec_bn_bias': 8.0,
     'L0_rec_bn_mean': 5.113,
     'L0_rec_bn_var': 8.0,
     'L0_rec_se_w1': 8.0,
     'L0_rec_se_w2': 8.0}
    for name, (base, spread) in spreads.items():
        noise = np.random.default_rng([zlib.crc32(name.encode()), seed]).standard_normal(out[name].shape)
        drawn = base * np.exp(spread * noise) if base else spread * noise
        out[name] = jnp.asarray(drawn.astype(out[name].dtype))
    for name, factor in factors.items():
        out[name] = (out[name] * factor).astype(out[name].dtype)
    return out
```

```python
import concourse.bass as bass
from concourse import mybir

BATCH, FIELDS, EMB = 2048, 40, 8
ROWS = FIELDS * EMB
HID1, HID2, RED = 1024, 512, 5
P = 128
HALF = 64
GROUPS = FIELDS // 8
GROUP_FIELDS = 8
NB = 512
BT = BATCH // NB
OT = HID1 // P
KT = 5
PHASES = 2
ROT = 8
CROSS = PHASES * ROT
WITHIN = 3
FULL = CROSS + WITHIN
LAST = FULL
LAST_K = [P, P, HALF]
WSTAGE = 4
SCRATCH = 4
BN_EPS = 1e-5

LEFT = [(0, 1), (0, 2), (3, 2)]
RIGHT = [(4, 4), (1, 3), (2, 3), (3, 2)]
CROSS_TILES = [(0, 0), (0, 2), (0, 3), (1, 1), (2, 0)]
NL, NR = len(LEFT), len(RIGHT)

WITHIN_TILES = [("step", dl, ((ph, g), (ph, g + 1))) for ph in range(PHASES) for dl in (1, 2, 3) for g in (0, 2)]
WITHIN_TILES += [("step", dl, ((0, 4), (1, 4))) for dl in (1, 2, 3)]
WITHIN_TILES += [("four", 0), ("four", 1), ("rest",)]


def deep_features(nc, xT, bn_main, bn_tail, wbl_rep, se1_main, se1_tail, se2_rep,
                  w1_full, w1_last, w1_last_tail, b1_cols, w2T, b2_cols, w3_cols, b3, out):
    f32, f32r = mybir.dt.float32, mybir.dt.float32r
    ALU, ACT = mybir.AluOpType, mybir.ActivationFunctionType
    from contextlib import ExitStack
    ds = bass.DynSlice

    t_tab = nc.dram_tensor("t_tab", (PHASES, BT, GROUPS, 2 * HALF, NB), f32, kind="Internal").ap()
    v_tab = nc.dram_tensor("v_tab", (PHASES, BT, GROUPS, HALF, NB), f32, kind="Internal").ap()

    with ExitStack() as ctx:
        def sb(name, shape, dt=f32):
            return ctx.enter_context(nc.sbuf_tensor(name, shape, dt))

        def sem(name):
            return ctx.enter_context(nc.semaphore(name))

        with nc.sbuf_tensor("v0t0", [P, 2, 3, BATCH], f32) as v0t0_space:
            v0t0 = v0t0_space
        scratch = sb("scratch", [P, SCRATCH, NB])
        phi = sb("phi", [P, 2, KT, NB], f32r)
        plo = sb("plo", [P, 2, KT, NB], f32r)
        whi = sb("whi", [P, OT, KT, P], f32r)
        wlo = sb("wlo", [P, OT, KT, P], f32r)
        wraw = sb("wraw", [P, WSTAGE, KT * P])
        acc = sb("acc", [P, OT, BATCH])
        ops = sb("ops", [P, 2 * NL + BT * NR, NB])
        bn = sb("bn", [P, 3, 4])
        bn_work = sb("bn_work", [P, 6, 3])
        b1s = sb("b1s", [P, OT])
        b2s = sb("b2s", [P, HID2 // P])
        w3s = sb("w3s", [P, HID2 // P])
        b3s = sb("b3s", [1, 1])
        bank = ctx.enter_context(nc.psum_tensor("bank", [P, 8, NB], f32))

        pre = 2 * NL + 3 * NR
        wbl_diag = ops[:, pre, 0:P]
        wbl_rows = ops[:, pre, P:P + EMB]
        se1 = ops[:, pre, 136:151].rearrange("p (k r) -> p k r", k=3)
        se2 = ops[0:RED, pre + 1, 0:ROWS]
        squeezed = ops[0:RED, pre + 2, :]
        v0, t0 = v0t0[:, 0], v0t0[:, 1]

        w2s = ops[:, 12:12 + OT, :]
        Q2 = HID2 // P

        def h2_tile(b, j):
            return ops[:, Q2 * (b % 2) + j, :]

        def y_row(b):
            return ops[0:1, 8 + b, :]

        def cols(b):
            return slice(b * NB, (b + 1) * NB)

        def gated(b, kind, blk, n=1):
            if b < 3:
                o, col = 3 * kind + blk, 1 + b
            elif blk < 2:
                o, col = 6 + blk, 2 + kind
            else:
                o, col = 6 + kind, 1
            return acc[:, o, cols(col)] if n == 1 else acc[:, o:o + n, cols(col)]

        x_in = [sem(f"x_in{b}") for b in range(BT)]
        small_cleared = sem("small_cleared")
        bn_in = sem("bn_in")
        se_in = sem("se_in")
        wbl_in = sem("wbl_in")
        diag_step = sem("diag_step")
        bn_step = sem("bn_step")
        bn_root = sem("bn_root")
        centred = sem("centred")
        v_ready = sem("v_ready")
        t_psum = sem("t_psum")
        t_ready = sem("t_ready")
        squeeze_psum = sem("squeeze_psum")
        squeeze_done = sem("squeeze_done")
        gate_psum = sem("gate_psum")
        gated_done = sem("gated_done")
        stored = [[sem(f"stored{ph}_{b}") for b in range(BT)] for ph in range(PHASES)]
        STORES = 9 * 16
        right_in = [sem(f"right_in{b}") for b in range(BT)]
        left_in = [sem(f"left_in{q}") for q in range(2)]
        LEFTS = 4 * 16
        within_in = [sem(f"within_in{q}") for q in range(2)]
        products = sem("products")
        p_hi = sem("p_hi")
        p_lo = sem("p_lo")
        w_in = [sem(f"w_in{s}") for s in range(WSTAGE)]
        w_hi = sem("w_hi")
        w_lo = sem("w_lo")
        group_done = sem("group_done")
        summed = sem("summed")
        tail_in = sem("tail_in")
        w2_in = sem("w2_in")
        h1_ready = sem("h1_ready")
        h2_psum = sem("h2_psum")
        h2_ready = sem("h2_ready")
        y_psum = sem("y_psum")
        y_ready = sem("y_ready")
        out_done = sem("out_done")

        block = ctx.enter_context(nc.Block())

        def slot(k, b):
            return k * BT + b

        def is_last(k):
            return isinstance(k, int) and k == LAST

        def tiles(k):
            return len(LAST_K) if is_last(k) else KT

        def features(k, b):
            return KT * BT * FULL + len(LAST_K) * b if is_last(k) else slot(k, b) * KT

        def following(k, b):
            return (k, b + 1) if b + 1 < BT else (k + 1, 0)

        def rows_of(k, t):
            return LAST_K[t] if is_last(k) else P

        def raw_feature(k, b, t):
            f = (len(LAST_K) if is_last(k) else KT) * b + t
            return scratch[0:rows_of(k, t), f % SCRATCH, :]

        def w_slices(k):
            return [(P, slice(0, 2)), (HALF, slice(2, 3))] if is_last(k) else [(P, slice(0, KT))]

        def w_loaded(k, o):
            return 16 * 2 * LAST + 32 * (o // WSTAGE + 1) if is_last(k) else 16 * (2 * k + o // WSTAGE + 1)

        @block.sync
        def _(sp):
            def store_tables(ph, b, v, t):
                for src, tab, copies in ((t, t_tab, 2), (v, v_tab, 1)):
                    for c in range(copies):
                        rows = slice(c * HALF, (c + 1) * HALF)
                        for h in range(2):
                            sp.dma_start(tab[ph, b, h:h + 3:2, rows, :].rearrange("g r n -> r g n"),
                                         src(0, 2)[h * HALF:(h + 1) * HALF]).then_inc(stored[ph][b], 16)
                        sp.dma_start(tab[ph, b, 4, rows, :], src(2, 1)[0:HALF]).then_inc(stored[ph][b], 16)

            def load_right(ph, b):
                for h in range(2):
                    for j in range(NR):
                        sp.dma_start(ops[h * HALF:(h + 1) * HALF, 2 * NL + b * NR + j, :],
                                     v_tab[ph, b, RIGHT[j][h], :, :]).then_inc(right_in[b], 16)

            def load_left(ph, c, b):
                for h, j, n in ((0, 0, 2), (0, 2, 1), (1, 0, 1), (1, 1, 2)):
                    src = t_tab[ph, b, LEFT[j][h], ds(c * EMB, HALF), :]
                    if n == 2:
                        src = src.unsqueeze(1).to_broadcast([HALF, 2, NB])
                    at = NL * (b % 2) + j
                    dst = ops[h * HALF:(h + 1) * HALF, at:at + n, :] if n == 2 else ops[h * HALF:(h + 1) * HALF, at, :]
                    sp.dma_start(dst, src).then_inc(left_in[b % 2], 16)

            def load_within(tile, b, left, right, signal):
                kind = tile[0]
                bs = b if isinstance(b, int) else ds(b, 1)

                def move(at, p0, rows, tab, r0, halves):
                    (ph, g), (ph1, _) = halves
                    for h, (ph, g) in enumerate(halves):
                        sp.dma_start(ops[h * HALF + p0:h * HALF + p0 + rows, at, :],
                                     tab[ph, bs, g, r0:r0 + rows, :] if isinstance(b, int)
                                     else tab[ph, bs, g, r0:r0 + rows, :].rearrange("b r n -> (b r) n")).then_inc(signal, 16)

                if kind == "step":
                    _, delta, halves = tile
                    n = HALF - EMB * delta
                    move(left, 0, n, t_tab, 0, halves)
                    move(left, n, HALF - n, t_tab, 0, halves)
                    move(right, 0, n, v_tab, EMB * delta, halves)
                    move(right, n, HALF - n, v_tab, n, halves)
                else:
                    quarters = [(tile[1], g) for g in range(4)] if kind == "four" else [(ph, 4) for ph in range(PHASES)]
                    for q, (ph, g) in enumerate(quarters):
                        at = slice(32 * q, 32 * q + 32)
                        sp.dma_start(ops[at, left, :], t_tab[ph, b, g, 0:32, :]).then_inc(signal, 16)
                        sp.dma_start(ops[at, right, :], v_tab[ph, b, g, 32:64, :]).then_inc(signal, 16)

            for b in range(BT):
                sp.dma_start(v0[:, 0:2, cols(b)], xT[0:2 * P, cols(b)].rearrange("(k p) n -> p k n", p=P)).then_inc(x_in[b], 16)
                sp.dma_start(v0[0:HALF, 2, cols(b)], xT[2 * P:ROWS, cols(b)]).then_inc(x_in[b], 16)

            for b in range(BT):
                sp.wait_ge(v_ready, 3 * (b + 1))
                sp.wait_ge(t_ready, 3 * (b + 1))
                store_tables(0, b, lambda blk, n: v0[:, blk:blk + n, cols(b)] if n > 1 else v0[:, blk, cols(b)],
                             lambda blk, n: t0[:, blk:blk + n, cols(b)] if n > 1 else t0[:, blk, cols(b)])
                if b == 1:
                    sp.wait_ge(stored[0][0], STORES)
                    load_right(0, 0)
                    load_left(0, 0, 0)
            sp.wait_ge(stored[0][1], STORES)
            load_right(0, 1)
            load_left(0, 0, 1)
            for b in range(BT):
                sp.wait_ge(gated_done, 6 * (b + 1))
                store_tables(1, b, lambda blk, n: gated(b, 0, blk, n), lambda blk, n: gated(b, 1, blk, n))

            for b in range(2, BT):
                sp.wait_ge(stored[0][b], STORES)
                load_right(0, b)
                sp.wait_ge(products, KT * (b - 1))
                load_left(0, 0, b)
            with sp.Fori(1, ROT) as c:
                for b in range(BT):
                    sp.wait_ge(products, KT * (slot(c, b) - 1))
                    load_left(0, c, b)
            for b in range(BT):
                sp.wait_ge(stored[1][b], STORES)
                sp.wait_ge(products, KT * slot(ROT - 1, b + 1))
                load_right(1, b)
                sp.wait_ge(products, KT * (slot(ROT, b) - 1))
                load_left(1, 0, b)
            with sp.Fori(1, ROT) as c:
                for b in range(BT):
                    sp.wait_ge(products, KT * (slot(c + ROT, b) - 1))
                    load_left(1, c, b)
            sp.wait_ge(products, KT * slot(CROSS, 0))
            for k in range(CROSS, FULL):
                with sp.Fori(0, BT // 2) as pair:
                    for q in range(2):
                        sp.wait_ge(products, KT * (pair * 2 + (slot(k, q) - 1)))
                        for t in range(KT):
                            load_within(WITHIN_TILES[(k - CROSS) * KT + t], pair * 2 + q,
                                        10 * q + t, 10 * q + KT + t, within_in[q])
            for b in range(BT):
                q = b % 2
                sp.wait_ge(products, features(LAST, 0) if b < 2 else features(LAST, b - 1))
                for t in range(len(LAST_K)):
                    load_within(WITHIN_TILES[WITHIN * KT + t], b, 6 * q + t, 6 * q + 3 + t, within_in[q])
            sp.dma_start(w2s, w2T.rearrange("(k p) n -> p k n", p=P)).then_inc(w2_in, 16)
            for b in range(BT):
                sp.wait_ge(y_ready, b + 1)
                sp.dma_start(out[b * NB:(b + 1) * NB, :].rearrange("n o -> o n"), y_row(b)).then_inc(out_done, 16)
            sp.wait_ge(out_done, 16 * BT)

        @block.gpsimd
        def _(pool):
            def load_w(k, o, wait=True):
                if wait:
                    pool.wait_ge(w_lo, k * OT + (o - WSTAGE + 1))
                s = o % WSTAGE
                if is_last(k):
                    pool.dma_start(wraw[:, s, 0:2 * P], w1_last[o, :, :]).then_inc(w_in[s], 16)
                    pool.dma_start(wraw[0:HALF, s, 2 * P:3 * P], w1_last_tail[o, :, :]).then_inc(w_in[s], 16)
                elif isinstance(k, int):
                    pool.dma_start(wraw[:, s, :], w1_full[k, o, :, :]).then_inc(w_in[s], 16)
                else:
                    pool.dma_start(wraw[:, s, :], w1_full[ds(k, 1), o, :, :].rearrange("k p n -> (k p) n")).then_inc(w_in[s], 16)

            nc.gpsimd.memset(bn[:], 1.0).then_inc(small_cleared, 1)
            pool.dma_start(wbl_rows, wbl_rep).then_inc(wbl_in, 16)
            pool.wait_ge(small_cleared, 1)
            pool.dma_start(bn[:, 0:2, :], bn_main).then_inc(bn_in, 16)
            pool.dma_start(bn[0:HALF, 2, :], bn_tail).then_inc(bn_in, 16)
            pool.dma_start(se1[:, 0:2, :], se1_main).then_inc(se_in, 16)
            pool.dma_start(se1[0:HALF, 2, :], se1_tail).then_inc(se_in, 16)
            pool.dma_start(se2, se2_rep).then_inc(se_in, 16)
            diag = wbl_diag.rearrange("p (i d) -> p i d", d=EMB)
            pool.wait_ge(wbl_in, 16)
            nc.gpsimd.tensor_copy(diag, wbl_rows.unsqueeze(1).to_broadcast([P, P // EMB, EMB])).then_inc(diag_step, 1)
            pool.wait_ge(diag_step, 1)
            nc.gpsimd.affine_select(out=diag, in_=diag, compare_op=ALU.is_ge, fill=0.0, base=0,
                                    pattern=[[-EMB, P // EMB], [0, EMB]], channel_multiplier=1).then_inc(diag_step, 1)
            pool.wait_ge(diag_step, 2)
            nc.gpsimd.affine_select(out=diag, in_=diag, compare_op=ALU.is_ge, fill=0.0, base=EMB - 1,
                                    pattern=[[EMB, P // EMB], [0, EMB]], channel_multiplier=-1).then_inc(diag_step, 1)
            for o in range(OT):
                load_w(0, o, wait=o >= WSTAGE)
            pool.dma_start(b1s[:], b1_cols).then_inc(tail_in, 16)
            pool.dma_start(b2s[:], b2_cols).then_inc(tail_in, 16)
            pool.dma_start(w3s[:], w3_cols).then_inc(tail_in, 16)
            pool.dma_start(b3s[:], b3).then_inc(tail_in, 16)
            with pool.Fori(1, FULL) as k:
                for o in range(OT):
                    load_w(k, o)
            for o in range(OT):
                load_w(LAST, o)

        @block.scalar
        def _(act):
            def round_w(k, o):
                act.wait_ge(w_in[o % WSTAGE], w_loaded(k, o))
                for rows, ts in w_slices(k):
                    src = wraw[0:rows, o % WSTAGE, :].rearrange("p (t n) -> p t n", t=KT)[:, ts, :]
                    last = nc.scalar.activation(whi[0:rows, o, ts, :], src, ACT.Copy)
                last.then_inc(w_hi, 1)

            def round_feature(k, b, t):
                act.wait_ge(products, features(k, b) + t + 1)
                nc.scalar.activation(phi[0:rows_of(k, t), b % 2, t, :], raw_feature(k, b, t), ACT.Copy).then_inc(p_hi, 1)

            def period(k, b, nxt):
                for o in range(OT):
                    if nxt and o < tiles(nxt[0]):
                        round_feature(*nxt, o)
                    if b == BT - 1 and not is_last(k):
                        act.wait_ge(group_done, slot(k, b) * OT + o + 1)
                        round_w(nxt[0], o)
                    if is_last(k):
                        act.wait_ge(summed, slot(k, b) * OT + o + 1)
                        h1 = acc[:, o, cols(b)]
                        nc.scalar.activation(h1, h1, ACT.Relu, bias=b1s[:, o:o + 1]).then_inc(h1_ready, 1)

            def chunk(k):
                for b in range(BT):
                    period(k, b, following(k, b))

            act.wait_ge(bn_step, 1)
            nc.scalar.activation(bn_work[:, 1, :], bn_work[:, 0, :], ACT.Sqrt).then_inc(bn_root, 1)
            for b in range(BT):
                for blk in range(3):
                    rows = P if blk < 2 else HALF
                    act.wait_ge(t_psum, 3 * b + blk + 1)
                    nc.scalar.activation(t0[0:rows, blk, cols(b)], bank[0:rows, blk, :], ACT.Copy).then_inc(t_ready, 1)
                for o in (2 * b, 2 * b + 1):
                    round_w(0, o)
            for t in range(KT):
                round_feature(0, 0, t)
            with act.Fori(0, FULL - 1) as k:
                chunk(k)
            chunk(FULL - 1)
            act.wait_ge(tail_in, 64)
            for b in range(BT):
                period(LAST, b, (LAST, b + 1) if b + 1 < BT else None)

            def relu2(b):
                for j in range(Q2):
                    act.wait_ge(h2_psum, Q2 * b + j + 1)
                    if b >= 2 and j == 0:
                        act.wait_ge(y_psum, b - 1)
                    nc.scalar.activation(h2_tile(b, j), bank[:, Q2 * (b % 2) + j, :], ACT.Relu,
                                         bias=b2s[:, j:j + 1]).then_inc(h2_ready, 1)

            def sigmoid(b):
                act.wait_ge(y_psum, b + 1)
                nc.scalar.activation(y_row(b), bank[0:1, Q2 * (b % 2) + Q2 - 1, :], ACT.Sigmoid,
                                     bias=b3s[:]).then_inc(y_ready, 1)

            relu2(0)
            for b in range(1, BT):
                relu2(b)
                sigmoid(b - 1)
            sigmoid(BT - 1)

        @block.vector
        def _(dve):
            def bn_op(n, emit):
                if n:
                    dve.wait_ge(bn_step, n)
                emit().then_inc(bn_step, 1)

            var_eps, root, inv, sq, corr, scale = (bn_work[:, i, :] for i in range(6))
            dve.wait_ge(bn_in, 32)
            bn_op(0, lambda: nc.vector.tensor_scalar(var_eps, bn[:, :, 3], BN_EPS, None, ALU.add))
            dve.wait_ge(bn_root, 1)
            bn_op(1, lambda: nc.vector.reciprocal(inv, root))
            bn_op(2, lambda: nc.vector.tensor_tensor(sq, inv, inv, ALU.mult))
            bn_op(3, lambda: nc.vector.tensor_tensor(corr, sq, var_eps, ALU.mult))
            bn_op(4, lambda: nc.vector.tensor_scalar(sq, corr, -0.5, 1.5, ALU.mult, ALU.add))
            bn_op(5, lambda: nc.vector.tensor_tensor(scale, inv, sq, ALU.mult))
            dve.wait_ge(bn_step, 6)
            for b in range(BT):
                dve.wait_ge(x_in[b], 32)
                for blk in range(3):
                    rows = P if blk < 2 else HALF
                    x = v0[0:rows, blk, cols(b)]
                    nc.vector.tensor_scalar(x, x, bn[0:rows, blk, 2:3], scale[0:rows, blk:blk + 1],
                                            ALU.subtract, ALU.mult).then_inc(centred, 1)
                for blk in range(3):
                    rows = P if blk < 2 else HALF
                    x = v0[0:rows, blk, cols(b)]
                    dve.wait_ge(centred, 3 * b + blk + 1)
                    nc.vector.tensor_scalar(x, x, bn[0:rows, blk, 0:1], bn[0:rows, blk, 1:2],
                                            ALU.mult, ALU.add).then_inc(v_ready, 1)

            def split_w(k, o):
                dve.wait_ge(w_hi, k * OT + o + 1)
                for rows, ts in w_slices(k):
                    src = wraw[0:rows, o % WSTAGE, :].rearrange("p (t n) -> p t n", t=KT)[:, ts, :]
                    last = nc.vector.tensor_tensor(wlo[0:rows, o, ts, :], src, whi[0:rows, o, ts, :].bitcast(f32),
                                                   ALU.subtract)
                last.then_inc(w_lo, 1)

            for b in range(BT):
                dve.wait_ge(squeeze_psum, b + 1)
                if b:
                    dve.wait_ge(gate_psum, 3 * b)
                nc.vector.tensor_scalar(squeezed, bank[0:RED, 3, :], 1.0 / EMB, 0.0, ALU.mult, ALU.max)\
                    .then_inc(squeeze_done, 1)
                dve.wait_ge(t_ready, 3 * (b + 1))
                for blk in range(3):
                    rows = P if blk < 2 else HALF
                    dve.wait_ge(gate_psum, 3 * b + blk + 1)
                    for kind, src in ((0, v0), (1, t0)):
                        nc.vector.scalar_tensor_tensor(gated(b, kind, blk)[0:rows], bank[0:rows, 4 + blk, :], 0.0,
                                                       src[0:rows, blk, cols(b)], ALU.max, ALU.mult)\
                            .then_inc(gated_done, 1)
                for o in (2 * b, 2 * b + 1):
                    split_w(0, o)

            def product(k, b, t, phase):
                rows = rows_of(k, t)
                if phase is None:
                    n = len(LAST_K) if is_last(k) else KT
                    base = 2 * n * (b % 2)
                    left, right = base + t, base + n + t
                    if t == 0:
                        full = 40 * 16
                        if is_last(k):
                            dve.wait_ge(within_in[b % 2], WITHIN * 2 * full + 20 * 16 * (b // 2 + 1))
                        else:
                            dve.wait_ge(within_in[b % 2], (k * 2 + (b // 2 + 1 - 2 * CROSS)) * full)
                else:
                    j, i = CROSS_TILES[t]
                    left, right = NL * (b % 2) + j, 2 * NL + b * NR + i
                    if t == 0:
                        dve.wait_ge(right_in[b], 2 * NR * 16 * (phase + 1))
                        dve.wait_ge(left_in[b % 2], (k * 2 + (b // 2 + 1)) * LEFTS)
                f = features(k, b) + t
                if not (isinstance(f, int) and f < SCRATCH):
                    dve.wait_ge(p_lo, f - (SCRATCH - 1))
                nc.vector.tensor_tensor(raw_feature(k, b, t), ops[0:rows, left, :], ops[0:rows, right, :],
                                        ALU.mult).then_inc(products, 1)

            def split_feature(k, b, t):
                rows = rows_of(k, t)
                dve.wait_ge(p_hi, features(k, b) + t + 1)
                nc.vector.tensor_tensor(plo[0:rows, b % 2, t, :], raw_feature(k, b, t),
                                        phi[0:rows, b % 2, t, :].bitcast(f32), ALU.subtract).then_inc(p_lo, 1)

            def add_sum(k, b, o, first):
                dve.wait_ge(group_done, slot(k, b) * OT + o + 1)
                dst = acc[:, o, cols(b)]
                if first:
                    if o == 0 and b:
                        dve.wait_ge(stored[1][b - 1], STORES)
                    if o == 6 and b == 1:
                        dve.wait_ge(stored[1][3], STORES)
                    nc.vector.tensor_copy(dst, bank[:, o, :]).then_inc(summed, 1)
                else:
                    nc.vector.tensor_tensor(dst, dst, bank[:, o, :], ALU.add).then_inc(summed, 1)

            def period(k, b, nxt, phase, first=False):
                for o in range(OT):
                    if nxt and o < tiles(nxt[0]):
                        product(*nxt, o, phase)
                    if nxt and 1 <= o <= tiles(nxt[0]):
                        split_feature(*nxt, o - 1)
                    if b == BT - 1 and nxt and o:
                        split_w(nxt[0], o - 1)
                    if b == 0 and o == 0 and not first:
                        split_w(k, OT - 1)
                    add_sum(k, b, o, first)

            def chunk(k, phase, next_phase, first=False):
                for b in range(BT):
                    period(k, b, following(k, b), phase if b + 1 < BT else next_phase, first)

            for b in range(BT):
                dve.wait_ge(stored[0][b], STORES)
            for t in range(KT):
                product(0, 0, t, 0)
                if t:
                    split_feature(0, 0, t - 1)
            split_feature(0, 0, KT - 1)
            chunk(0, 0, 0, first=True)
            with dve.Fori(1, ROT - 1) as k:
                chunk(k, 0, 0)
            chunk(ROT - 1, 0, 1)
            with dve.Fori(ROT, CROSS - 1) as k:
                chunk(k, 1, 1)
            chunk(CROSS - 1, 1, None)
            with dve.Fori(CROSS, FULL - 1) as k:
                chunk(k, None, None)
            chunk(FULL - 1, None, None)
            for b in range(BT):
                period(LAST, b, (LAST, b + 1) if b + 1 < BT else None, None)

        @block.tensor
        def _(pe):
            def project(b):
                for blk in range(3):
                    rows = P if blk < 2 else HALF
                    pe.wait_ge(v_ready, 3 * b + blk + 1)
                    if b:
                        pe.wait_ge(t_ready, 3 * (b - 1) + blk + 1)
                    nc.tensor.matmul(bank[0:rows, blk, :], wbl_diag[0:rows, 0:rows], v0[0:rows, blk, cols(b)],
                                     start=True, stop=True).then_inc(t_psum, 1)

            def squeeze(b):
                if b:
                    pe.wait_ge(squeeze_done, b)
                for blk in range(3):
                    rows = P if blk < 2 else HALF
                    last = nc.tensor.matmul(bank[0:RED, 3, :], se1[0:rows, blk, :], v0[0:rows, blk, cols(b)],
                                            start=blk == 0, stop=blk == 2)
                last.then_inc(squeeze_psum, 1)

            def excite(b):
                pe.wait_ge(squeeze_done, b + 1)
                for blk in range(3):
                    rows = P if blk < 2 else HALF
                    if b:
                        pe.wait_ge(gated_done, 6 * (b - 1) + 2 * blk + 2)
                    nc.tensor.matmul(bank[0:rows, 4 + blk, :], se2[:, blk * P:blk * P + rows], squeezed,
                                     start=True, stop=True).then_inc(gate_psum, 1)

            pe.wait_ge(diag_step, 3)
            pe.wait_ge(se_in, 48)
            for b in range(BT):
                project(b)
                if b:
                    excite(b - 1)
                squeeze(b)
            excite(BT - 1)

            def chunk(k, first=False):
                for b in range(BT):
                    for o in range(OT):
                        if not (first and b == 0):
                            pe.wait_ge(summed, slot(k, b) * OT + (o + 1 - OT))
                        elif o == 0:
                            pe.wait_ge(t_ready, 3 * BT)
                            pe.wait_ge(squeeze_done, BT)
                            pe.wait_ge(gated_done, 6 * BT)
                        if b == 0:
                            pe.wait_ge(w_lo, k * OT + o + 1)
                        n = tiles(k)
                        for t in range(n):
                            if o == 0:
                                pe.wait_ge(p_lo, features(k, b) + t + 1)
                            rows = rows_of(k, t)
                            hi, lo = phi[0:rows, b % 2, t, :], plo[0:rows, b % 2, t, :]
                            nc.tensor.matmul(bank[:, o, :], whi[0:rows, o, t, :], hi, start=t == 0, stop=False)
                            nc.tensor.matmul(bank[:, o, :], whi[0:rows, o, t, :], lo, start=False, stop=False)
                            last = nc.tensor.matmul(bank[:, o, :], wlo[0:rows, o, t, :], hi, start=False, stop=t == n - 1)
                        last.then_inc(group_done, 1)

            chunk(0, first=True)
            with pe.Fori(1, FULL) as k:
                chunk(k)
            chunk(LAST)

            def layer2(b):
                for j in range(Q2):
                    at = Q2 * (b % 2) + j
                    if b < 2:
                        pe.wait_ge(summed, slot(LAST, BT - 1) * OT + at + 1)
                    else:
                        pe.wait_ge(h2_ready, Q2 * (b - 2) + j + 1)
                        if j == Q2 - 1:
                            pe.wait_ge(y_ready, b - 1)
                    for kk in range(OT):
                        if j == 0:
                            pe.wait_ge(h1_ready, OT * b + kk + 1)
                        last = nc.tensor.matmul(bank[:, at, :], w2s[:, kk, j * P:(j + 1) * P], acc[:, kk, cols(b)],
                                                start=kk == 0, stop=kk == OT - 1)
                    last.then_inc(h2_psum, 1)

            def layer3(b):
                pe.wait_ge(h2_ready, Q2 * (b + 1))
                for j in range(Q2):
                    last = nc.tensor.matmul(bank[0:1, Q2 * (b % 2) + Q2 - 1, :], w3s[:, j:j + 1], h2_tile(b, j),
                                            start=j == 0, stop=j == Q2 - 1)
                last.then_inc(y_psum, 1)

            pe.wait_ge(w2_in, 16)
            pe.wait_ge(tail_in, 64)
            layer2(0)
            for b in range(1, BT):
                layer2(b)
                layer3(b - 1)
            layer3(BT - 1)



def feature_columns():
    import itertools
    import numpy as np
    pair = {p: n for n, p in enumerate(itertools.combinations(range(FIELDS), 2))}

    def column(phase, i, j, d):
        return ((0 if phase else len(pair)) + pair[i, j]) * EMB + d

    order = []
    for phase in range(PHASES):
        for c in range(ROT):
            for j, i in CROSS_TILES:
                for h in range(2):
                    for r in range(GROUP_FIELDS):
                        left = GROUP_FIELDS * LEFT[j][h] + (r + c) % GROUP_FIELDS
                        right = GROUP_FIELDS * RIGHT[i][h] + r
                        order += [column(phase, left, right, d) for d in range(EMB)]
    for tile in WITHIN_TILES:
        if tile[0] == "step":
            for phase, g in tile[2]:
                for r in range(GROUP_FIELDS - tile[1]):
                    order += [column(phase, 8 * g + r, 8 * g + r + tile[1], d) for d in range(EMB)]
                for r in range(tile[1]):
                    order += [column(phase, 8 * g + r, 8 * g + r + 8 - tile[1], d) for d in range(EMB)]
        else:
            for phase, g in ([(tile[1], g) for g in range(4)] if tile[0] == "four" else [(0, 4), (1, 4)]):
                for r in range(4):
                    order += [column(phase, 8 * g + r, 8 * g + r + 4, d) for d in range(EMB)]
    return np.array(order)


def kernel(**inputs):
    import numpy as np
    import concourse.bacc as bacc
    from concourse import mybir as mb
    from concourse.bass_utils import run_bass_kernel_spmd

    def get(name):
        return np.asarray(inputs["L0_rec_" + name])

    order = feature_columns()
    w1T = get("d_w1").T[order]
    cut = FULL * KT * P
    bn_rows = np.stack([get("bn_weight"), get("bn_bias"), get("bn_mean"), get("bn_var")], axis=1)
    se1_rows = np.repeat(get("se_w1").T, EMB, axis=0)

    def by_block(a):
        return a[:2 * P].reshape(2, P, -1).transpose(1, 0, 2)

    arrays = {
        "xT": np.asarray(inputs["r_emb"]).T,
        "bn_main": by_block(bn_rows), "bn_tail": bn_rows[2 * P:],
        "wbl_rep": np.tile(get("w_bl").T, (P // EMB, 1)),
        "se1_main": by_block(se1_rows), "se1_tail": se1_rows[2 * P:],
        "se2_rep": np.repeat(get("se_w2").T, EMB, axis=1),
        "w1_full": w1T[:cut].reshape(FULL, KT, P, OT, P).transpose(0, 3, 2, 1, 4).reshape(FULL, OT, P, KT * P),
        "w1_last": w1T[cut:cut + 2 * P].reshape(2, P, OT, P).transpose(2, 1, 0, 3).reshape(OT, P, 2 * P),
        "w1_last_tail": w1T[cut + 2 * P:].reshape(HALF, OT, P).transpose(1, 0, 2),
        "b1_cols": get("d_b1").reshape(OT, P).T,
        "w2T": get("d_w2").T,
        "b2_cols": get("d_b2").reshape(HID2 // P, P).T,
        "w3_cols": get("d_w3").reshape(HID2 // P, P).T,
        "b3": get("d_b3").reshape(1, 1),
    }
    nc = bacc.Bacc("TRN2", target_bir_lowering=False, num_devices=1)
    arrays = {n: np.ascontiguousarray(a) for n, a in arrays.items()}
    args = {n: nc.dram_tensor(n, a.shape, mb.dt.from_np(a.dtype), kind="ExternalInput").ap() for n, a in arrays.items()}
    out = nc.dram_tensor("out", (BATCH, 1), mb.dt.float32, kind="ExternalOutput").ap()
    deep_features(nc, out=out, **args)
    ran = run_bass_kernel_spmd(nc, [arrays], core_ids=[0])
    return ran.results[0]["out"]
```

```python
import concourse.bass as bass
from concourse import mybir

BATCH, FIELDS, EMB = 2048, 40, 8
ROWS = FIELDS * EMB
HID1, HID2, RED = 1024, 512, 5
P = 128
HALF = 64
GROUPS = FIELDS // 8
GROUP_FIELDS = 8
NB = 512
BT = BATCH // NB
OT = HID1 // P
KT = 5
PHASES = 2
ROT = 8
CROSS = PHASES * ROT
WITHIN = 3
FULL = CROSS + WITHIN
LAST = FULL
LAST_K = [P, P, HALF]
WSTAGE = 4
SCRATCH = 4
BN_EPS = 1e-5

LEFT = [(0, 1), (0, 2), (3, 2)]
RIGHT = [(4, 4), (1, 3), (2, 3), (3, 2)]
CROSS_TILES = [(0, 0), (0, 2), (0, 3), (1, 1), (2, 0)]
NL, NR = len(LEFT), len(RIGHT)

WITHIN_TILES = [("step", dl, ((ph, g), (ph, g + 1))) for ph in range(PHASES) for dl in (1, 2, 3) for g in (0, 2)]
WITHIN_TILES += [("step", dl, ((0, 4), (1, 4))) for dl in (1, 2, 3)]
WITHIN_TILES += [("four", 0), ("four", 1), ("rest",)]


def deep_features(nc, xT, bn_main, bn_tail, wbl_rep, se1_main, se1_tail, se2_rep,
                  w1_full, w1_last, w1_last_tail, b1_cols, w2T, b2_cols, w3_cols, b3, out):
    f32, f32r = mybir.dt.float32, mybir.dt.float32r
    ALU, ACT = mybir.AluOpType, mybir.ActivationFunctionType
    from contextlib import ExitStack
    ds = bass.DynSlice

    t_tab = nc.dram_tensor("t_tab", (PHASES, BT, GROUPS, 2 * HALF, NB), f32, kind="Internal").ap()
    v_tab = nc.dram_tensor("v_tab", (PHASES, BT, GROUPS, HALF, NB), f32, kind="Internal").ap()

    with ExitStack() as ctx:
        def sb(name, shape, dt=f32):
            return ctx.enter_context(nc.sbuf_tensor(name, shape, dt))

        def sem(name):
            return ctx.enter_context(nc.semaphore(name))

        scratch = sb("scratch", [P, SCRATCH, NB])
        phi = sb("phi", [P, 2, KT, NB], f32r)
        plo = sb("plo", [P, 2, KT, NB], f32r)
        whi = sb("whi", [P, OT, KT, P], f32r)
        wlo = sb("wlo", [P, OT, KT, P], f32r)
        wraw = sb("wraw", [P, WSTAGE, KT * P])
        acc = sb("acc", [P, OT, BATCH])
        with nc.sbuf_tensor("h1_parts", [P, 2 * NL + BT * NR, NB], f32r) as space:
            h1_parts = space
        ops = sb("ops", [P, 2 * NL + BT * NR, NB])
        bn = sb("bn", [P, 3, 4])
        bn_work = sb("bn_work", [P, 6, 3])
        b1s = sb("b1s", [P, OT])
        b2s = sb("b2s", [P, HID2 // P])
        w3s = sb("w3s", [P, HID2 // P])
        b3s = sb("b3s", [1, 1])
        ones = sb("ones", [P, 1])
        bank = ctx.enter_context(nc.psum_tensor("bank", [P, 8, NB], f32))

        pre = 2 * NL + 3 * NR
        wbl_diag = ops[:, pre, 0:P]
        wbl_rows = ops[:, pre, P:P + EMB]
        se1 = ops[:, pre, 136:151].rearrange("p (k r) -> p k r", k=3)
        se2 = ops[0:RED, pre + 1, 0:ROWS]
        squeezed = [ops[0:RED, pre + 2 + i, :] for i in range(2)]
        LO_AT, HI2_AT = 32, 64
        gate_at = 2 * NL + 2 * NR
        squeezed_parts = [h1_parts[:, gate_at + i, :] for i in range(2)]
        se2_parts = h1_parts[:, gate_at + 2, 0:3 * P]

        Q2 = HID2 // P
        W2_AT = 12
        H1_RING = (2 * NL + BT * NR) // 2

        def h1_part(b, k, part):
            return h1_parts[:, 2 * ((b * OT + k) % H1_RING) + part, :]

        def w2_store(k, part):
            if k < 4:
                return (phi, plo)[part][:, k // 2, 3 + k % 2, :]
            o = 2 * (k - 4)
            return (whi, wlo)[part][:, o:o + 2, 3:5, :]

        def w2_tile(k, part, j):
            if k < 4:
                return w2_store(k, part)[:, j * P:(j + 1) * P]
            return (whi, wlo)[part][:, 2 * (k - 4) + j // 2, 3 + j % 2, :]

        def w2_raw(k):
            raw = ops[:, W2_AT + k, :]
            return raw if k < 4 else raw.rearrange("p (a t n) -> p a t n", a=2, t=2)

        def h2_tile(b, j):
            return wraw[:, j, 0:NB] if b % 2 else scratch[:, j, :]

        def weighted_h2(b):
            return acc[:, 1, cols(b)]

        def y_row(b):
            return acc[0:1, 0, cols(b)]

        def cols(b):
            return slice(b * NB, (b + 1) * NB)

        CELLS = [[((0, 1), (2, 1)), ((3, 1), (5, 1))],
                 [((0, 2), (6, 1)), ((2, 2), (7, 1))],
                 [((4, 2), (0, 3)), ((6, 2), (1, 3))],
                 [((2, 3), (4, 3)), ((5, 3), (7, 3))]]
        V, T = 0, 1

        def cell(b, kind, blk, n=1):
            o, col = CELLS[b][kind][blk // 2]
            o += blk % 2
            return acc[:, o, cols(col)] if n == 1 else acc[:, o:o + n, cols(col)]

        x_in = [sem(f"x_in{b}") for b in range(BT)]
        small_cleared = sem("small_cleared")
        parts_cleared = sem("parts_cleared")
        se2_hi = sem("se2_hi")
        se2_lo = sem("se2_lo")
        bn_in = sem("bn_in")
        se_in = sem("se_in")
        wbl_in = sem("wbl_in")
        diag_step = sem("diag_step")
        bn_step = sem("bn_step")
        bn_root = sem("bn_root")
        centred = sem("centred")
        v_ready = sem("v_ready")
        t_psum = sem("t_psum")
        t_ready = sem("t_ready")
        squeeze_psum = sem("squeeze_psum")
        squeeze_done = sem("squeeze_done")
        squeezed_hi = sem("squeezed_hi")
        squeezed_lo = sem("squeezed_lo")
        gate_psum = sem("gate_psum")
        gated_done = sem("gated_done")
        stored = [[sem(f"stored{ph}_{b}") for b in range(BT)] for ph in range(PHASES)]
        STORES = 9 * 16
        right_in = [sem(f"right_in{b}") for b in range(BT)]
        left_in = [sem(f"left_in{q}") for q in range(2)]
        first_left_in = [sem(f"first_left_in{b}") for b in range(2)]
        LEFTS = 4 * 16
        within_in = [sem(f"within_in{q}") for q in range(2)]
        products = sem("products")
        p_hi = sem("p_hi")
        p_lo = sem("p_lo")
        w_in = [sem(f"w_in{s}") for s in range(WSTAGE)]
        w_hi = sem("w_hi")
        w_lo = sem("w_lo")
        group_done = sem("group_done")
        summed = sem("summed")
        tail_in = sem("tail_in")
        w2_in = sem("w2_in")
        w2_hi = sem("w2_hi")
        w2_lo = sem("w2_lo")
        h1_relu = sem("h1_relu")
        h1_hi = sem("h1_hi")
        h1_lo = sem("h1_lo")
        h1_used = sem("h1_used")
        h2_psum = sem("h2_psum")
        h2_ready = sem("h2_ready")
        weighted = sem("weighted")
        ones_set = sem("ones_set")
        y_psum = sem("y_psum")
        y_ready = sem("y_ready")
        out_done = sem("out_done")

        block = ctx.enter_context(nc.Block())

        def slot(k, b):
            return k * BT + b

        def is_last(k):
            return isinstance(k, int) and k == LAST

        def tiles(k):
            return len(LAST_K) if is_last(k) else KT

        def features(k, b):
            return KT * BT * FULL + len(LAST_K) * b if is_last(k) else slot(k, b) * KT

        def following(k, b):
            return (k, b + 1) if b + 1 < BT else (k + 1, 0)

        def rows_of(k, t):
            return LAST_K[t] if is_last(k) else P

        def raw_feature(k, b, t):
            f = (len(LAST_K) if is_last(k) else KT) * b + t
            return scratch[0:rows_of(k, t), f % SCRATCH, :]

        def w_slices(k):
            return [(P, slice(0, 2)), (HALF, slice(2, 3))] if is_last(k) else [(P, slice(0, KT))]

        def w_loaded(k, o):
            return 16 * 2 * LAST + 32 * (o // WSTAGE + 1) if is_last(k) else 16 * (2 * k + o // WSTAGE + 1)

        @block.sync
        def _(sp):
            def store_tables(ph, b):
                for kind, tab, copies in ((T, t_tab, 2), (V, v_tab, 1)):
                    for c in range(copies):
                        rows = slice(c * HALF, (c + 1) * HALF)
                        for h in range(2):
                            sp.dma_start(tab[ph, b, h:h + 3:2, rows, :].rearrange("g r n -> r g n"),
                                         cell(b, kind, 0, 2)[h * HALF:(h + 1) * HALF]).then_inc(stored[ph][b], 16)
                        sp.dma_start(tab[ph, b, 4, rows, :], cell(b, kind, 2)[0:HALF]).then_inc(stored[ph][b], 16)

            def load_right(ph, b):
                for h in range(2):
                    for j in range(NR):
                        sp.dma_start(ops[h * HALF:(h + 1) * HALF, 2 * NL + b * NR + j, :],
                                     v_tab[ph, b, RIGHT[j][h], :, :]).then_inc(right_in[b], 16)

            def load_left(ph, c, b):
                for h, j, n in ((0, 0, 2), (0, 2, 1), (1, 0, 1), (1, 1, 2)):
                    src = t_tab[ph, b, LEFT[j][h], ds(c * EMB, HALF), :]
                    if n == 2:
                        src = src.unsqueeze(1).to_broadcast([HALF, 2, NB])
                    at = NL * (b % 2) + j
                    dst = ops[h * HALF:(h + 1) * HALF, at:at + n, :] if n == 2 else ops[h * HALF:(h + 1) * HALF, at, :]
                    sp.dma_start(dst, src).then_inc(left_in[b % 2], 16)

            def load_within(tile, b, left, right, signal):
                kind = tile[0]
                bs = b if isinstance(b, int) else ds(b, 1)

                def move(at, p0, rows, tab, r0, halves):
                    for h, (ph, g) in enumerate(halves):
                        sp.dma_start(ops[h * HALF + p0:h * HALF + p0 + rows, at, :],
                                     tab[ph, bs, g, r0:r0 + rows, :] if isinstance(b, int)
                                     else tab[ph, bs, g, r0:r0 + rows, :].rearrange("b r n -> (b r) n")).then_inc(signal, 16)

                if kind == "step":
                    _, delta, halves = tile
                    n = HALF - EMB * delta
                    move(left, 0, n, t_tab, 0, halves)
                    move(left, n, HALF - n, t_tab, 0, halves)
                    move(right, 0, n, v_tab, EMB * delta, halves)
                    move(right, n, HALF - n, v_tab, n, halves)
                else:
                    quarters = [(tile[1], g) for g in range(4)] if kind == "four" else [(ph, 4) for ph in range(PHASES)]
                    for q, (ph, g) in enumerate(quarters):
                        at = slice(32 * q, 32 * q + 32)
                        sp.dma_start(ops[at, left, :], t_tab[ph, b, g, 0:32, :]).then_inc(signal, 16)
                        sp.dma_start(ops[at, right, :], v_tab[ph, b, g, 32:64, :]).then_inc(signal, 16)

            for b in range(BT):
                sp.dma_start(cell(b, V, 0, 2), xT[0:2 * P, cols(b)].rearrange("(k p) n -> p k n", p=P)).then_inc(x_in[b], 16)
                sp.dma_start(cell(b, V, 2)[0:HALF], xT[2 * P:ROWS, cols(b)]).then_inc(x_in[b], 16)

            def copy_blocks(b, at, kind, blocks, signal):
                for j, (g0, g1) in enumerate(blocks):
                    if (g0 % 2, g1) == (0, g0 + 1):
                        sp.dma_start(ops[:, at + j, :], cell(b, kind, g0 // 2)).then_inc(signal, 32)
                    else:
                        for h, g in enumerate((g0, g1)):
                            sp.dma_start(ops[h * HALF:(h + 1) * HALF, at + j, :],
                                         cell(b, kind, g // 2)[g % 2 * HALF:(g % 2 + 1) * HALF]).then_inc(signal, 16)

            for b in range(BT):
                sp.wait_ge(v_ready, 3 * (b + 1))
                if b < 2:
                    copy_blocks(b, 2 * NL + b * NR, V, RIGHT, right_in[b])
                sp.wait_ge(t_ready, 3 * (b + 1))
                if b < 2:
                    copy_blocks(b, NL * b, T, LEFT, first_left_in[b])
                store_tables(0, b)
            sp.wait_ge(stored[0][2], STORES)
            sp.wait_ge(products, KT)
            load_left(0, 0, 2)
            for b in range(BT):
                sp.wait_ge(gated_done, 6 * (b + 1))
                if b == BT - 1:
                    load_right(0, 2)
                store_tables(1, b)
            sp.wait_ge(stored[0][3], STORES)
            load_right(0, 3)
            sp.wait_ge(products, KT * 2)
            load_left(0, 0, 3)
            with sp.Fori(1, ROT) as c:
                for b in range(BT):
                    sp.wait_ge(products, KT * (slot(c, b) - 1))
                    load_left(0, c, b)
            for b in range(BT):
                sp.wait_ge(stored[1][b], STORES)
                sp.wait_ge(products, KT * slot(ROT - 1, b + 1))
                load_right(1, b)
                sp.wait_ge(products, KT * (slot(ROT, b) - 1))
                load_left(1, 0, b)
            with sp.Fori(1, ROT) as c:
                for b in range(BT):
                    sp.wait_ge(products, KT * (slot(c + ROT, b) - 1))
                    load_left(1, c, b)
            sp.wait_ge(products, KT * slot(CROSS, 0))
            for k in range(CROSS, FULL):
                with sp.Fori(0, BT // 2) as pair:
                    for q in range(2):
                        sp.wait_ge(products, KT * (pair * 2 + (slot(k, q) - 1)))
                        for t in range(KT):
                            load_within(WITHIN_TILES[(k - CROSS) * KT + t], pair * 2 + q,
                                        10 * q + t, 10 * q + KT + t, within_in[q])
            for b in range(BT):
                q = b % 2
                sp.wait_ge(products, features(LAST, 0) if b < 2 else features(LAST, b - 1))
                for t in range(len(LAST_K)):
                    load_within(WITHIN_TILES[WITHIN * KT + t], b, 6 * q + t, 6 * q + 3 + t, within_in[q])
                if b == 1:
                    sp.dma_start(ops[:, W2_AT:W2_AT + OT, :], w2T.rearrange("(k p) n -> p k n", p=P)).then_inc(w2_in, 16)
            for b in range(BT):
                sp.wait_ge(y_ready, b + 1)
                sp.dma_start(out[b * NB:(b + 1) * NB, :].rearrange("n o -> o n"), y_row(b)).then_inc(out_done, 16)
            sp.wait_ge(out_done, 16 * BT)

        @block.gpsimd
        def _(pool):
            def load_w(k, o, wait=True):
                if wait:
                    pool.wait_ge(w_lo, k * OT + (o - WSTAGE + 1))
                s = o % WSTAGE
                if is_last(k):
                    pool.dma_start(wraw[:, s, 0:2 * P], w1_last[o, :, :]).then_inc(w_in[s], 16)
                    pool.dma_start(wraw[0:HALF, s, 2 * P:3 * P], w1_last_tail[o, :, :]).then_inc(w_in[s], 16)
                elif isinstance(k, int):
                    pool.dma_start(wraw[:, s, :], w1_full[k, o, :, :]).then_inc(w_in[s], 16)
                else:
                    pool.dma_start(wraw[:, s, :], w1_full[ds(k, 1), o, :, :].rearrange("k p n -> (k p) n")).then_inc(w_in[s], 16)

            pool.dma_start(wbl_rows, wbl_rep).then_inc(wbl_in, 16)
            pool.dma_start(se1[:, 0:2, :], se1_main).then_inc(se_in, 16)
            pool.dma_start(se1[0:HALF, 2, :], se1_tail).then_inc(se_in, 16)
            pool.dma_start(se2, se2_rep).then_inc(se_in, 16)
            diag = wbl_diag.rearrange("p (i d) -> p i d", d=EMB)
            pool.wait_ge(wbl_in, 16)
            nc.gpsimd.tensor_copy(diag, wbl_rows.unsqueeze(1).to_broadcast([P, P // EMB, EMB])).then_inc(diag_step, 1)
            pool.wait_ge(diag_step, 1)
            nc.gpsimd.affine_select(out=diag, in_=diag, compare_op=ALU.is_ge, fill=0.0, base=0,
                                    pattern=[[-EMB, P // EMB], [0, EMB]], channel_multiplier=1).then_inc(diag_step, 1)
            pool.wait_ge(diag_step, 2)
            nc.gpsimd.affine_select(out=diag, in_=diag, compare_op=ALU.is_ge, fill=0.0, base=EMB - 1,
                                    pattern=[[EMB, P // EMB], [0, EMB]], channel_multiplier=-1).then_inc(diag_step, 1)
            for o in range(OT):
                load_w(0, o, wait=o >= WSTAGE)
            pool.dma_start(b1s[:], b1_cols).then_inc(tail_in, 16)
            pool.dma_start(b2s[:], b2_cols).then_inc(tail_in, 16)
            pool.dma_start(w3s[:], w3_cols).then_inc(tail_in, 16)
            pool.dma_start(b3s[:], b3).then_inc(tail_in, 16)
            with pool.Fori(1, FULL) as k:
                for o in range(OT):
                    load_w(k, o)
            for o in range(OT):
                load_w(LAST, o)

        @block.scalar
        def _(act):
            def round_w(k, o):
                act.wait_ge(w_in[o % WSTAGE], w_loaded(k, o))
                for rows, ts in w_slices(k):
                    src = wraw[0:rows, o % WSTAGE, :].rearrange("p (t n) -> p t n", t=KT)[:, ts, :]
                    last = nc.scalar.activation(whi[0:rows, o, ts, :], src, ACT.Copy)
                    if rows == HALF:
                        last = nc.scalar.activation(whi[HALF:P, o, ts, :], src, ACT.Copy)
                last.then_inc(w_hi, 1)

            def round_feature(k, b, t):
                act.wait_ge(products, features(k, b) + t + 1)
                nc.scalar.activation(phi[0:rows_of(k, t), b % 2, t, :], raw_feature(k, b, t), ACT.Copy).then_inc(p_hi, 1)

            def round_h1(b, k):
                if b * OT + k >= H1_RING:
                    act.wait_ge(h1_used, b * OT + k - H1_RING + 1)
                nc.scalar.activation(h1_part(b, k, 0), acc[:, k, cols(b)], ACT.Copy).then_inc(h1_hi, 1)

            def period(k, b, nxt, first=False):
                for o in range(OT):
                    if first and o + 1 < BT:
                        round_squeezed(o + 1)
                    if nxt and o < tiles(nxt[0]):
                        round_feature(*nxt, o)
                    if first and o + WSTAGE < OT:
                        round_w(0, o + WSTAGE)
                    if b == BT - 1 and not is_last(k):
                        act.wait_ge(group_done, slot(k, b) * OT + o + 1)
                        round_w(nxt[0], o)
                    if is_last(k):
                        act.wait_ge(summed, slot(k, b) * OT + o + 1)
                        h1 = acc[:, o, cols(b)]
                        nc.scalar.activation(h1, h1, ACT.Relu, bias=b1s[:, o:o + 1]).then_inc(h1_relu, 1)
                        if b == 1:
                            if o == 0:
                                act.wait_ge(w2_in, 16)
                            nc.scalar.activation(w2_store(o, 0), w2_raw(o), ACT.Copy).then_inc(w2_hi, 1)
                        if b == BT - 1:
                            if o == 0:
                                act.wait_ge(w2_lo, OT)
                                act.wait_ge(h1_relu, OT)
                            round_h1(0, o)

            def chunk(k, first=False):
                for b in range(BT):
                    period(k, b, following(k, b), first and b == 0)

            act.wait_ge(small_cleared, 1)
            act.dma_start(bn[:, 0:2, :], bn_main).then_inc(bn_in, 16)
            act.dma_start(bn[0:HALF, 2, :], bn_tail).then_inc(bn_in, 16)
            act.wait_ge(bn_step, 1)
            nc.scalar.activation(bn_work[:, 1, :], bn_work[:, 0, :], ACT.Sqrt).then_inc(bn_root, 1)
            for b in range(BT):
                for blk in range(3):
                    rows = P if blk < 2 else HALF
                    act.wait_ge(t_psum, 3 * b + blk + 1)
                    nc.scalar.activation(cell(b, T, blk)[0:rows], bank[0:rows, blk, :], ACT.Copy).then_inc(t_ready, 1)
                round_w(0, b)

            def round_squeezed(b):
                act.wait_ge(squeeze_done, b + 1)
                if b >= 2:
                    act.wait_ge(gate_psum, 3 * (b - 1))
                for at in (0, HI2_AT):
                    nc.scalar.activation(squeezed_parts[b % 2][at:at + RED], squeezed[b % 2], ACT.Copy)\
                        .then_inc(squeezed_hi, 1)

            act.wait_ge(se_in, 48)
            act.wait_ge(parts_cleared, 1)
            for at in (0, LO_AT):
                nc.scalar.activation(se2_parts[at:at + RED, 0:ROWS], se2, ACT.Copy).then_inc(se2_hi, 1)
            for t in range(KT):
                round_feature(0, 0, t)
            round_squeezed(0)
            chunk(0, first=True)
            with act.Fori(1, FULL - 1) as k:
                chunk(k)
            chunk(FULL - 1)
            act.wait_ge(tail_in, 64)
            for b in range(BT):
                period(LAST, b, (LAST, b + 1) if b + 1 < BT else None)

            def relu2(b):
                for j in range(Q2):
                    if j < Q2 - 1:
                        act.wait_ge(h2_psum, (Q2 - 1) * b + j + 1)
                    else:
                        act.wait_ge(h1_used, OT * (b + 1))
                    if b >= 2 and j == 0:
                        act.wait_ge(weighted, Q2 * (b - 1))
                    nc.scalar.activation(h2_tile(b, j), bank[:, Q2 * (b % 2) + j, :], ACT.Relu,
                                         bias=b2s[:, j:j + 1]).then_inc(h2_ready, 1)

            def sigmoid(b):
                act.wait_ge(y_psum, b + 1)
                nc.scalar.activation(y_row(b), bank[0:1, Q2 * (b % 2) + Q2 - 1, :], ACT.Sigmoid,
                                     bias=b3s[:]).then_inc(y_ready, 1)

            for b in range(BT):
                if b + 1 < BT:
                    act.wait_ge(h1_relu, OT * (b + 2))
                    for k in range(OT):
                        round_h1(b + 1, k)
                relu2(b)
                if b:
                    sigmoid(b - 1)
            sigmoid(BT - 1)

        @block.vector
        def _(dve):
            def bn_op(n, emit):
                if n:
                    dve.wait_ge(bn_step, n)
                emit().then_inc(bn_step, 1)

            var_eps, root, inv, sq, corr, scale = (bn_work[:, i, :] for i in range(6))
            nc.vector.memset(bn[:], 1.0).then_inc(small_cleared, 1)
            nc.vector.memset(ones[:], 1.0).then_inc(ones_set, 1)
            nc.vector.memset(h1_parts[:, gate_at:gate_at + 3, :].bitcast(f32), 0.0).then_inc(parts_cleared, 1)
            dve.wait_ge(bn_in, 32)
            bn_op(0, lambda: nc.vector.tensor_scalar(var_eps, bn[:, :, 3], BN_EPS, None, ALU.add))
            dve.wait_ge(bn_root, 1)
            bn_op(1, lambda: nc.vector.reciprocal(inv, root))
            bn_op(2, lambda: nc.vector.tensor_tensor(sq, inv, inv, ALU.mult))
            bn_op(3, lambda: nc.vector.tensor_tensor(corr, sq, var_eps, ALU.mult))
            bn_op(4, lambda: nc.vector.tensor_scalar(sq, corr, -0.5, 1.5, ALU.mult, ALU.add))
            bn_op(5, lambda: nc.vector.tensor_tensor(scale, inv, sq, ALU.mult))
            dve.wait_ge(bn_step, 6)
            for b in range(BT):
                dve.wait_ge(x_in[b], 32)
                for blk in range(3):
                    rows = P if blk < 2 else HALF
                    x = cell(b, V, blk)[0:rows]
                    nc.vector.tensor_scalar(x, x, bn[0:rows, blk, 2:3], scale[0:rows, blk:blk + 1],
                                            ALU.subtract, ALU.mult).then_inc(centred, 1)
                for blk in range(3):
                    rows = P if blk < 2 else HALF
                    x = cell(b, V, blk)[0:rows]
                    dve.wait_ge(centred, 3 * b + blk + 1)
                    nc.vector.tensor_scalar(x, x, bn[0:rows, blk, 0:1], bn[0:rows, blk, 1:2],
                                            ALU.mult, ALU.add).then_inc(v_ready, 1)

            def split_w(k, o):
                dve.wait_ge(w_hi, k * OT + o + 1)
                for rows, ts in w_slices(k):
                    src = wraw[0:rows, o % WSTAGE, :].rearrange("p (t n) -> p t n", t=KT)[:, ts, :]
                    last = nc.vector.tensor_tensor(wlo[0:rows, o, ts, :], src, whi[0:rows, o, ts, :].bitcast(f32),
                                                   ALU.subtract)
                last.then_inc(w_lo, 1)

            def squeeze(b):
                dve.wait_ge(squeeze_psum, b + 1)
                if b >= 2:
                    dve.wait_ge(squeezed_lo, b - 1)
                nc.vector.tensor_scalar(squeezed[b % 2], bank[0:RED, 4, :], 1.0 / EMB, 0.0, ALU.mult, ALU.max)\
                    .then_inc(squeeze_done, 1)

            def split_squeezed(b):
                dve.wait_ge(squeezed_hi, 2 * (b + 1))
                nc.vector.tensor_tensor(squeezed_parts[b % 2][LO_AT:LO_AT + RED], squeezed[b % 2],
                                        squeezed_parts[b % 2][0:RED].bitcast(f32), ALU.subtract).then_inc(squeezed_lo, 1)

            def gate(b):
                dve.wait_ge(stored[0][b], STORES)
                if b < 2:
                    dve.wait_ge(right_in[b], 2 * NR * 16)
                    dve.wait_ge(first_left_in[b], 2 * NL * 16)
                for blk in range(3):
                    rows = P if blk < 2 else HALF
                    dve.wait_ge(gate_psum, 3 * b + blk + 1)
                    for kind in (V, T):
                        x = cell(b, kind, blk)[0:rows]
                        nc.vector.scalar_tensor_tensor(x, bank[0:rows, 5 + blk, :], 0.0, x, ALU.max, ALU.mult)\
                            .then_inc(gated_done, 1)

            def product(k, b, t, phase):
                rows = rows_of(k, t)
                if phase is None:
                    n = len(LAST_K) if is_last(k) else KT
                    base = 2 * n * (b % 2)
                    left, right = base + t, base + n + t
                    if t == 0:
                        full = 40 * 16
                        if is_last(k):
                            dve.wait_ge(within_in[b % 2], WITHIN * 2 * full + 20 * 16 * (b // 2 + 1))
                        else:
                            dve.wait_ge(within_in[b % 2], (k * 2 + (b // 2 + 1 - 2 * CROSS)) * full)
                else:
                    j, i = CROSS_TILES[t]
                    left, right = NL * (b % 2) + j, 2 * NL + b * NR + i
                    if t == 0:
                        dve.wait_ge(right_in[b], 2 * NR * 16 * (phase + 1))
                        if isinstance(k, int) and slot(k, b) < 2:
                            dve.wait_ge(first_left_in[b], 2 * NL * 16)
                        else:
                            dve.wait_ge(left_in[b % 2], (k * 2 + b // 2) * LEFTS)
                f = features(k, b) + t
                if not (isinstance(f, int) and f < SCRATCH):
                    dve.wait_ge(p_lo, f - (SCRATCH - 1))
                nc.vector.tensor_tensor(raw_feature(k, b, t), ops[0:rows, left, :], ops[0:rows, right, :],
                                        ALU.mult).then_inc(products, 1)

            def split_feature(k, b, t):
                rows = rows_of(k, t)
                dve.wait_ge(p_hi, features(k, b) + t + 1)
                out = phi[HALF:P, b % 2, t, :] if rows == HALF else plo[:, b % 2, t, :]
                nc.vector.tensor_tensor(out, raw_feature(k, b, t), phi[0:rows, b % 2, t, :].bitcast(f32),
                                        ALU.subtract).then_inc(p_lo, 1)

            def add_sum(k, b, o, first):
                dve.wait_ge(group_done, slot(k, b) * OT + o + 1)
                dst = acc[:, o, cols(b)]
                if first:
                    if o == 0 and b:
                        dve.wait_ge(stored[1][b - 1], STORES)
                        if b > 1:
                            dve.wait_ge(stored[1][b], STORES)
                    if o == 6 and b == 1:
                        dve.wait_ge(stored[1][1], STORES)
                    nc.vector.tensor_copy(dst, bank[:, o, :]).then_inc(summed, 1)
                else:
                    nc.vector.tensor_tensor(dst, dst, bank[:, o, :], ALU.add).then_inc(summed, 1)

            def split_h1(b, k):
                dve.wait_ge(h1_hi, b * OT + k + 1)
                nc.vector.tensor_tensor(h1_part(b, k, 1), acc[:, k, cols(b)], h1_part(b, k, 0).bitcast(f32),
                                        ALU.subtract).then_inc(h1_lo, 1)

            def period(k, b, nxt, phase, first=False):
                for o in range(OT):
                    start = first and b == 0
                    if start:
                        if o + 2 < OT:
                            split_w(0, o + 2)
                        add_sum(k, b, o, first)
                        if o + 1 < BT:
                            squeeze(o + 1)
                        if o < BT:
                            gate(o)
                        if o + 1 < BT:
                            split_squeezed(o + 1)
                    if nxt and o < tiles(nxt[0]):
                        product(*nxt, o, phase)
                    if nxt and 1 <= o <= tiles(nxt[0]):
                        split_feature(*nxt, o - 1)
                    if b == BT - 1 and nxt and o:
                        split_w(nxt[0], o - 1)
                    if b == 0 and o == 0 and not first:
                        split_w(k, OT - 1)
                    if not start:
                        add_sum(k, b, o, first)
                    if is_last(k) and b == 2:
                        dve.wait_ge(w2_hi, o + 1)
                        nc.vector.tensor_tensor(w2_store(o, 1), w2_raw(o), w2_store(o, 0).bitcast(f32),
                                                ALU.subtract).then_inc(w2_lo, 1)
                    if is_last(k) and b == BT - 1:
                        split_h1(0, o)

            def chunk(k, phase, next_phase, first=False):
                for b in range(BT):
                    period(k, b, following(k, b), phase if b + 1 < BT else next_phase, first)

            for o in range(2):
                split_w(0, o)
            for t in range(KT):
                product(0, 0, t, 0)
                if t:
                    split_feature(0, 0, t - 1)
            split_feature(0, 0, KT - 1)
            squeeze(0)
            dve.wait_ge(parts_cleared, 1)
            dve.wait_ge(se2_hi, 2)
            nc.vector.tensor_tensor(se2_parts[HI2_AT:HI2_AT + RED, 0:ROWS], se2, se2_parts[0:RED, 0:ROWS].bitcast(f32),
                                    ALU.subtract).then_inc(se2_lo, 1)
            split_squeezed(0)
            chunk(0, 0, 0, first=True)
            with dve.Fori(1, ROT - 1) as k:
                chunk(k, 0, 0)
            chunk(ROT - 1, 0, 1)
            with dve.Fori(ROT, CROSS - 1) as k:
                chunk(k, 1, 1)
            chunk(CROSS - 1, 1, None)
            with dve.Fori(CROSS, FULL - 1) as k:
                chunk(k, None, None)
            chunk(FULL - 1, None, None)
            for b in range(BT):
                period(LAST, b, (LAST, b + 1) if b + 1 < BT else None, None)
            dve.wait_ge(tail_in, 64)
            for b in range(BT):
                if b + 1 < BT:
                    for k in range(OT):
                        split_h1(b + 1, k)
                for j in range(Q2):
                    dve.wait_ge(h2_ready, Q2 * b + j + 1)
                    z = weighted_h2(b)
                    if j == 0:
                        nc.vector.tensor_scalar(z, h2_tile(b, j), w3s[:, j:j + 1], None, ALU.mult).then_inc(weighted, 1)
                    else:
                        dve.wait_ge(weighted, Q2 * b + j)
                        nc.vector.scalar_tensor_tensor(z, h2_tile(b, j), w3s[:, j:j + 1], z, ALU.mult, ALU.add)\
                            .then_inc(weighted, 1)

        @block.tensor
        def _(pe):
            def project(b):
                for blk in range(3):
                    rows = P if blk < 2 else HALF
                    pe.wait_ge(v_ready, 3 * b + blk + 1)
                    if b:
                        pe.wait_ge(t_ready, 3 * (b - 1) + blk + 1)
                    nc.tensor.matmul(bank[0:rows, blk, :], wbl_diag[0:rows, 0:rows], cell(b, V, blk)[0:rows],
                                     start=True, stop=True).then_inc(t_psum, 1)

            def squeeze(b):
                if b:
                    pe.wait_ge(squeeze_done, b)
                for blk in range(3):
                    rows = P if blk < 2 else HALF
                    last = nc.tensor.matmul(bank[0:RED, 4, :], se1[0:rows, blk, :], cell(b, V, blk)[0:rows],
                                            start=blk == 0, stop=blk == 2)
                last.then_inc(squeeze_psum, 1)

            def excite(b):
                pe.wait_ge(squeezed_lo, b + 1)
                for blk in range(3):
                    if b:
                        pe.wait_ge(gated_done, 6 * (b - 1) + 2 * blk + 2)
                    nc.tensor.matmul(bank[:, 5 + blk, :], se2_parts[:, blk * P:(blk + 1) * P], squeezed_parts[b % 2],
                                     start=True, stop=True).then_inc(gate_psum, 1)

            pe.wait_ge(diag_step, 3)
            pe.wait_ge(se_in, 48)
            for b in range(BT):
                project(b)
            squeeze(0)

            def chunk(k, first=False):
                for b in range(BT):
                    for o in range(OT):
                        if not (first and b == 0):
                            pe.wait_ge(summed, slot(k, b) * OT + (o + 1 - OT))
                        elif o == 0:
                            pe.wait_ge(t_ready, 3 * BT)
                        elif o == 4:
                            pe.wait_ge(squeeze_done, BT)
                        elif o == 5:
                            pe.wait_ge(gated_done, 6 * BT)
                        if b == 0:
                            pe.wait_ge(w_lo, k * OT + o + 1)
                        n = tiles(k)
                        for t in range(n):
                            if o == 0:
                                pe.wait_ge(p_lo, features(k, b) + t + 1)
                            rows = rows_of(k, t)
                            hi, lo = phi[0:rows, b % 2, t, :], plo[0:rows, b % 2, t, :]
                            if rows == HALF:
                                nc.tensor.matmul(bank[:, o, :], whi[:, o, t, :], phi[:, b % 2, t, :], start=False, stop=False)
                            else:
                                nc.tensor.matmul(bank[:, o, :], whi[:, o, t, :], hi, start=t == 0, stop=False)
                                nc.tensor.matmul(bank[:, o, :], whi[:, o, t, :], lo, start=False, stop=False)
                            last = nc.tensor.matmul(bank[:, o, :], wlo[0:rows, o, t, :], hi, start=False, stop=t == n - 1)
                        last.then_inc(group_done, 1)
                        if first and b == 0 and o + 1 < BT:
                            squeeze(o + 1)
                        if first and b == 0 and o < BT:
                            if o == 0:
                                pe.wait_ge(se2_lo, 1)
                            excite(o)

            chunk(0, first=True)
            with pe.Fori(1, FULL) as k:
                chunk(k)
            chunk(LAST)

            def bank2(b, j):
                return bank[:, Q2 * (b % 2) + j, :]

            def free_bank2(b, j):
                if b < 2:
                    pe.wait_ge(summed, slot(LAST, BT - 1) * OT + Q2 * b + j + 1)
                else:
                    pe.wait_ge(h2_ready, Q2 * (b - 2) + j + 1)
                    if j == Q2 - 1:
                        pe.wait_ge(y_ready, b - 1)

            def products2(b, j, k):
                hi, lo = h1_part(b, k, 0), h1_part(b, k, 1)
                nc.tensor.matmul(bank2(b, j), w2_tile(k, 0, j), hi, start=k == 0, stop=False)
                nc.tensor.matmul(bank2(b, j), w2_tile(k, 0, j), lo, start=False, stop=False)
                return nc.tensor.matmul(bank2(b, j), w2_tile(k, 1, j), hi, start=False, stop=k == OT - 1)

            def layer2(b):
                for k in range(OT):
                    pe.wait_ge(h1_lo, OT * b + k + 1)
                    for j in range(Q2):
                        if k == 0:
                            free_bank2(b, j)
                        last = products2(b, j, k)
                        if k == OT - 1 and j < Q2 - 1:
                            last.then_inc(h2_psum, 1)
                    last.then_inc(h1_used, 1)

            def layer2_last(b):
                pe.wait_ge(h1_lo, OT * (b + 1))
                for j in range(Q2):
                    free_bank2(b, j)
                    for k in range(OT):
                        last = products2(b, j, k)
                    if j < Q2 - 1:
                        last.then_inc(h2_psum, 1)
                last.then_inc(h1_used, OT)

            def layer3(b):
                pe.wait_ge(weighted, Q2 * (b + 1))
                nc.tensor.matmul(bank2(b, Q2 - 1)[0:1], ones[:], weighted_h2(b), start=True, stop=True)\
                    .then_inc(y_psum, 1)

            pe.wait_ge(w2_lo, OT)
            pe.wait_ge(ones_set, 1)
            layer2(0)
            for b in range(1, BT):
                (layer2_last if b == BT - 1 else layer2)(b)
                layer3(b - 1)
            layer3(BT - 1)



def feature_columns():
    import itertools
    import numpy as np
    pair = {p: n for n, p in enumerate(itertools.combinations(range(FIELDS), 2))}

    def column(phase, i, j, d):
        return ((0 if phase else len(pair)) + pair[i, j]) * EMB + d

    order = []
    for phase in range(PHASES):
        for c in range(ROT):
            for j, i in CROSS_TILES:
                for h in range(2):
                    for r in range(GROUP_FIELDS):
                        left = GROUP_FIELDS * LEFT[j][h] + (r + c) % GROUP_FIELDS
                        right = GROUP_FIELDS * RIGHT[i][h] + r
                        order += [column(phase, left, right, d) for d in range(EMB)]
    for tile in WITHIN_TILES:
        if tile[0] == "step":
            for phase, g in tile[2]:
                for r in range(GROUP_FIELDS - tile[1]):
                    order += [column(phase, 8 * g + r, 8 * g + r + tile[1], d) for d in range(EMB)]
                for r in range(tile[1]):
                    order += [column(phase, 8 * g + r, 8 * g + r + 8 - tile[1], d) for d in range(EMB)]
        else:
            for phase, g in ([(tile[1], g) for g in range(4)] if tile[0] == "four" else [(0, 4), (1, 4)]):
                for r in range(4):
                    order += [column(phase, 8 * g + r, 8 * g + r + 4, d) for d in range(EMB)]
    return np.array(order)


def kernel(**inputs):
    import numpy as np
    import concourse.bacc as bacc
    from concourse import mybir as mb
    from concourse.bass_utils import run_bass_kernel_spmd

    def get(name):
        return np.asarray(inputs["L0_rec_" + name])

    order = feature_columns()
    w1T = get("d_w1").T[order]
    cut = FULL * KT * P
    bn_rows = np.stack([get("bn_weight"), get("bn_bias"), get("bn_mean"), get("bn_var")], axis=1)
    se1_rows = np.repeat(get("se_w1").T, EMB, axis=0)

    def by_block(a):
        return a[:2 * P].reshape(2, P, -1).transpose(1, 0, 2)

    arrays = {
        "xT": np.asarray(inputs["r_emb"]).T,
        "bn_main": by_block(bn_rows), "bn_tail": bn_rows[2 * P:],
        "wbl_rep": np.tile(get("w_bl").T, (P // EMB, 1)),
        "se1_main": by_block(se1_rows), "se1_tail": se1_rows[2 * P:],
        "se2_rep": np.repeat(get("se_w2").T, EMB, axis=1),
        "w1_full": w1T[:cut].reshape(FULL, KT, P, OT, P).transpose(0, 3, 2, 1, 4).reshape(FULL, OT, P, KT * P),
        "w1_last": w1T[cut:cut + 2 * P].reshape(2, P, OT, P).transpose(2, 1, 0, 3).reshape(OT, P, 2 * P),
        "w1_last_tail": w1T[cut + 2 * P:].reshape(HALF, OT, P).transpose(1, 0, 2),
        "b1_cols": get("d_b1").reshape(OT, P).T,
        "w2T": get("d_w2").T,
        "b2_cols": get("d_b2").reshape(HID2 // P, P).T,
        "w3_cols": get("d_w3").reshape(HID2 // P, P).T,
        "b3": get("d_b3").reshape(1, 1),
    }
    nc = bacc.Bacc("TRN2", target_bir_lowering=False, num_devices=1)
    arrays = {n: np.ascontiguousarray(a) for n, a in arrays.items()}
    args = {n: nc.dram_tensor(n, a.shape, mb.dt.from_np(a.dtype), kind="ExternalInput").ap() for n, a in arrays.items()}
    out = nc.dram_tensor("out", (BATCH, 1), mb.dt.float32, kind="ExternalOutput").ap()
    deep_features(nc, out=out, **args)
    ran = run_bass_kernel_spmd(nc, [arrays], core_ids=[0])
    return ran.results[0]["out"]
```
